# Optimizing a Trainium2 kernel written in Bass

```python
import numpy as np
import jax
import jax.numpy as jnp

def _softmax(x, axis=-1):
    return jax.nn.softmax(x, axis=axis)

def _gelu(x):
    return jax.nn.gelu(x, approximate=True)

def _silu(x):
    return jax.nn.silu(x)

def _sigmoid(x):
    return jax.nn.sigmoid(x)

def _layernorm(x, axis=-1, eps=1e-05):
    m = jnp.mean(x, axis=axis, keepdims=True)
    v = jnp.var(x, axis=axis, keepdims=True)
    return (x - m) / jnp.sqrt(v + eps)

def _scatter_add(tgt, idx, src, axis=0):
    return tgt.at[idx].add(src)

def _segment_sum(src, seg, n):
    return jax.ops.segment_sum(src, seg, n)
kernel_name = 'mk_cond_resid_d2_seqx_r2_fed422'

def setup_inputs(seed: int=0):
    np.random.seed(seed)
    _w = jnp.asarray

    def _rec_inputs():
        import jax
        import jax.numpy as jnp
        _rk = jax.random.key(seed)
        x = -7.109e-05 + 0.9999 * jax.random.normal(jax.random.fold_in(_rk, 1), (64, 128, 2048), jnp.float32)
        _lenS = 128 - jax.random.randint(jax.random.fold_in(_rk, 7), (64,), 0, max(1, 128 // 4) + 1, jnp.int32)
        _lenS2 = 128 - jax.random.randint(jax.random.fold_in(_rk, 8), (64,), 0, max(1, 128 // 4) + 1, jnp.int32)
        itok_B_0_30 = jax.random.randint(jax.random.fold_in(_rk, 11), (64,), 0, 31, jnp.int32)
        itok_B_0_15 = jax.random.randint(jax.random.fold_in(_rk, 12), (64,), 0, 16, jnp.int32)
        return (x, itok_B_0_30, itok_B_0_15)
    x, itok_B_0_30, itok_B_0_15 = _rec_inputs()

    def _L0_cond_setup():
        import jax, jax.numpy as jnp
        import numpy as np
        B, C, D, T, S = (64, 128, 128, 2048, 32)
        key = jax.random.key(seed)
        k1, k2, k3 = jax.random.split(key, 3)
        x = jax.random.normal(k1, (B, C, T), dtype=jnp.float32)
        subjects = jax.random.randint(k2, (B,), 0, S, dtype=jnp.int64)
        weights = jax.random.normal(k3, (S, C, D), dtype=jnp.float32) * (1.0 / np.sqrt(C))
        return {'x': x, 'subjects': subjects, 'weights': weights}
    _L0_cond_all = _L0_cond_setup()
    _L0_cond_in = {k: v for k, v in _L0_cond_all.items() if k in ('weights',)}
    del _L0_cond_all

    def _L1_cond_setup():
        import jax, jax.numpy as jnp
        import numpy as np
        B, C, T = (64, 128, 2048)
        S, D = (16, 128)
        key = jax.random.key(seed)
        k1, k2, k3 = jax.random.split(key, 3)
        x = jax.random.normal(k1, (B, C, T), dtype=jnp.float32)
        condition = jax.random.randint(k2, (B,), 0, S, dtype=jnp.int64)
        bound = float(np.sqrt(6.0 / C))
        weights = jax.random.uniform(k3, (S, C, D), dtype=jnp.float32, minval=-bound, maxval=bound)
        return {'x': x, 'condition': condition, 'weights': weights}
    _L1_cond_all = _L1_cond_setup()
    _L1_cond_in = {k: v for k, v in _L1_cond_all.items() if k in ('weights',)}
    del _L1_cond_all
    return {'x': x, 'itok_B_0_30': itok_B_0_30, 'itok_B_0_15': itok_B_0_15, 'L0_cond_weights': _L0_cond_in['weights'], 'L1_cond_weights': _L1_cond_in['weights']}

def reference(x, itok_B_0_30, itok_B_0_15, L0_cond_weights, L1_cond_weights):
    import jax
    import jax.numpy as jnp

    def _L0_cond_ref(x, subjects, weights):
        import jax, jax.numpy as jnp
        import numpy as np
        B, C, D, T, S = (64, 128, 128, 2048, 32)
        w = weights[subjects]
        return jnp.einsum('bct,bcd->bdt', x, w)

    def _L1_cond_ref(x, condition, weights):
        import jax, jax.numpy as jnp
        import numpy as np
        B, C, T = (64, 128, 2048)
        S, D = (16, 128)
        W = weights[condition]
        return jnp.einsum('bct,bcd->bdt', x, W)
    x = x + _L0_cond_ref(x, itok_B_0_30, L0_cond_weights)
    x = x + _L1_cond_ref(x, itok_B_0_15, L1_cond_weights)
    return x

_drawn_inputs = setup_inputs


def setup_inputs(seed=0):
    import zlib

    import numpy as np

    out = dict(_drawn_inputs(seed))
    spreads = {}
    factors = {}
    for name, (base, spread) in spreads.items():
        noise = np.random.default_rng([zlib.crc32(name.encode()), seed]).standard_normal(out[name].shape)
        drawn = base * np.exp(spread * noise) if base else spread * noise
        out[name] = jnp.asarray(drawn.astype(out[name].dtype))
    for name, factor in factors.items():
        out[name] = (out[name] * factor).astype(out[name].dtype)
    return out
```

```python
import concourse.bass as bass
from concourse import mybir
from contextlib import ExitStack


def cond_resid_kernel(nc, x, subj, cond, w0, w1, out):
    f32 = mybir.dt.float32
    ALU = mybir.AluOpType
    ACT = mybir.ActivationFunctionType

    BATCH, C, T = x.shape
    S0, S1 = w0.shape[0], w1.shape[0]
    BANK = 512
    HALF = T // 2
    SLOTS = 8
    TURNS = BATCH // SLOTS
    PER_BANK = BANK // C
    TGROUPS = S0 // PER_BANK
    W0_PARTS = 4
    PART = S0 // W0_PARTS
    assert C == 128 and HALF == 2 * BANK and BATCH == TURNS * SLOTS and S0 == TGROUPS * PER_BANK
    assert PART % PER_BANK == 0

    w0_c = w0.rearrange("s c d -> c s d")
    w1_c = w1.rearrange("s c d -> c s d")

    ctx = ExitStack()
    with ctx:
        def sb(name, shape, dt=f32):
            return ctx.enter_context(nc.sbuf_tensor(name, shape, dt))

        def sem(name):
            return ctx.enter_context(nc.semaphore(name))

        xs = sb("xs", [C, SLOTS, T])
        w0_sb = sb("w0_sb", [C, S0, C])
        w0T_sb = sb("w0T_sb", [C, S0, C])
        w1_sb = sb("w1_sb", [C, S1, C])
        subj_sb = sb("subj_sb", [1, BATCH], subj.dtype)
        cond_sb = sb("cond_sb", [1, BATCH], cond.dtype)
        ident = sb("ident", [C, C])
        aT = sb("aT", [C, 2, C])
        bw = sb("bw", [C, 2, C])
        ab_sum = sb("ab_sum", [C, 2, C])
        m = sb("m", [C, 2, C])

        ps_x = ctx.enter_context(nc.psum_tensor("ps_x", [C, 2, HALF], f32))
        ps_ab = ctx.enter_context(nc.psum_tensor("ps_ab", [C, 2, BANK], f32))

        idx_in = sem("idx_in")
        w0_in = [sem(f"w0_in{p}") for p in range(W0_PARTS)]
        w1_in = sem("w1_in")
        x_in = [sem(f"x_in{s}") for s in range(SLOTS)]
        x_out = [sem(f"x_out{s}") for s in range(SLOTS)]
        ident_zero = sem("ident_zero")
        ident_done = sem("ident_done")
        turned = sem("turned")
        turned_out = sem("turned_out")
        picked = sem("picked")
        ab_done = sem("ab_done")
        m_done = sem("m_done")
        half_done = sem("half_done")
        half_added = sem("half_added")

        block = ctx.enter_context(nc.Block())

        @block.sync
        def _(sp):
            for p in range(W0_PARTS):
                sp.dma_start(w0_sb[:, p * PART:(p + 1) * PART, :],
                             w0_c[:, p * PART:(p + 1) * PART, :]).then_inc(w0_in[p], 16)
            sp.dma_start(w1_sb[:, :, :], w1_c).then_inc(w1_in, 16)
            for s in range(SLOTS):
                sp.dma_start(xs[:, s, :], x[s, :, :]).then_inc(x_in[s], 16)
            with sp.Fori(1, TURNS) as t:
                for s in range(SLOTS):
                    sp.wait_ge(x_out[s], 16 * t)
                    src = x[bass.ds(t * SLOTS + s, 1), :, :].rearrange("a c t -> c (a t)")
                    sp.dma_start(xs[:, s, :], src).then_inc(x_in[s], 16)

        @block.gpsimd
        def _(pool):
            nc.gpsimd.memset(ident[:, :], 0.0).then_inc(ident_zero, 1)
            pool.wait_ge(ident_zero, 1)
            nc.gpsimd.affine_select(out=ident[:, :], in_=ident[:, :], compare_op=ALU.not_equal, fill=1.0, base=0,
                                    pattern=[[-1, C]], channel_multiplier=1).then_inc(ident_done, 1)

            def pick(b, k):
                i = pool.value_load(subj_sb[0:1, bass.ds(b, 1)], min_val=0, max_val=S0 - 1)
                j = pool.value_load(cond_sb[0:1, bass.ds(b, 1)], min_val=0, max_val=S1 - 1)
                a = w0_sb[:, bass.ds(i, 1), :].rearrange("c a d -> c (a d)")
                at = w0T_sb[:, bass.ds(i, 1), :].rearrange("c a d -> c (a d)")
                bb = w1_sb[:, bass.ds(j, 1), :].rearrange("c a d -> c (a d)")
                nc.gpsimd.tensor_copy(aT[:, k % 2, :], at).then_inc(picked, 1)
                nc.gpsimd.tensor_copy(bw[:, k % 2, :], bb).then_inc(picked, 1)
                nc.gpsimd.tensor_tensor(ab_sum[:, k % 2, :], a, bb, ALU.add).then_inc(picked, 1)

            pool.wait_ge(idx_in, 32)
            for p in range(W0_PARTS):
                pool.wait_ge(w0_in[p], 16)
            pool.wait_ge(w1_in, 16)
            pool.wait_ge(turned_out, TGROUPS)
            for k in range(2):
                pick(k, k)
            with pool.Fori(1, BATCH // 2) as u:
                for k in range(2):
                    pool.wait_ge(m_done, u * 2 + (k - 1))
                    pick(u * 2 + k, k)

        @block.tensor
        def _(pe):
            pe.wait_ge(ident_done, 1)
            for g in range(TGROUPS):
                first = g * PER_BANK
                if first % PART == 0:
                    pe.wait_ge(w0_in[first // PART], 16)
                if g >= 4:
                    pe.wait_ge(turned_out, g - 3)
                bank = ps_x[:, g // 2 % 2, g % 2 * BANK:(g % 2 + 1) * BANK]
                for n in range(PER_BANK):
                    last = nc.tensor.transpose(bank[:, n * C:(n + 1) * C], w0_sb[:, first + n, :], ident[:, :])
                last.then_inc(turned, 1)

            def product_ab(b, k):
                pe.wait_ge(picked, b * 3 + 3)
                nc.tensor.matmul(ps_ab[:, k % 2, 0:C], aT[:, k % 2, :], bw[:, k % 2, :],
                                 start=True, stop=True).then_inc(ab_done, 1)

            def product_x(t, s, first):
                b = t * SLOTS + s
                pe.wait_ge(m_done, b + 1)
                pe.wait_ge(x_in[s], t * 16 + 16)
                for h in range(2):
                    if not (first and s == 0):
                        pe.wait_ge(half_added, b * 2 + (h - 1))
                    for n in range(2):
                        col = h * HALF + n * BANK
                        last = nc.tensor.matmul(ps_x[:, h, n * BANK:(n + 1) * BANK], m[:, s % 2, :],
                                                xs[:, s, col:col + BANK], start=True, stop=True)
                    last.then_inc(half_done, 1)

            def turn(t, first=False, final=False):
                for s in range(SLOTS):
                    if not (final and s == SLOTS - 1):
                        product_ab(t * SLOTS + (s + 1), s + 1)
                    product_x(t, s, first)

            pe.wait_ge(turned_out, TGROUPS)
            product_ab(0, 0)
            turn(0, first=True)
            with pe.Fori(1, TURNS - 1) as t:
                turn(t)
            turn(TURNS - 1, final=True)

        @block.vector
        def _(dve):
            def make_m(b, k, reused):
                dve.wait_ge(ab_done, b + 1)
                dve.wait_ge(picked, b * 3 + 3)
                if reused:
                    dve.wait_ge(half_done, b * 2 - 2)
                nc.vector.tensor_tensor(m[:, k % 2, :], ps_ab[:, k % 2, 0:C], ab_sum[:, k % 2, :],
                                        ALU.add).then_inc(m_done, 1)

            def add_x(t, s):
                b = t * SLOTS + s
                for h in range(2):
                    dve.wait_ge(half_done, b * 2 + (h + 1))
                    xh = xs[:, s, h * HALF:(h + 1) * HALF]
                    nc.vector.tensor_tensor(xh, ps_x[:, h, :], xh, ALU.add).then_inc(half_added, 1)

            def turn(t, first=False, final=False):
                for s in range(SLOTS):
                    if not (final and s == SLOTS - 1):
                        make_m(t * SLOTS + (s + 1), s + 1, reused=not (first and s == 0))
                    add_x(t, s)

            make_m(0, 0, reused=False)
            turn(0, first=True)
            with dve.Fori(1, TURNS - 1) as t:
                turn(t)
            turn(TURNS - 1, final=True)

        @block.scalar
        def _(act):
            act.dma_start(subj_sb[:, :], subj.rearrange("(a n) -> a n", a=1)).then_inc(idx_in, 16)
            act.dma_start(cond_sb[:, :], cond.rearrange("(a n) -> a n", a=1)).then_inc(idx_in, 16)
            for g in range(TGROUPS):
                act.wait_ge(turned, g + 1)
                bank = ps_x[:, g // 2 % 2, g % 2 * BANK:(g % 2 + 1) * BANK]
                dst = w0T_sb[:, g * PER_BANK:(g + 1) * PER_BANK, :].rearrange("c s d -> c (s d)")
                nc.scalar.activation(dst, bank, ACT.Copy).then_inc(turned_out, 1)
            with act.Fori(0, TURNS) as t:
                for s in range(SLOTS):
                    b = t * SLOTS + s
                    act.wait_ge(half_added, b * 2 + 2)
                    dst = out[bass.ds(b, 1), :, :].rearrange("a c t -> c (a t)")
                    act.dma_start(dst, xs[:, s, :]).then_inc(x_out[s], 16)
            for s in range(SLOTS):
                act.wait_ge(x_out[s], 16 * TURNS)


def kernel(x, itok_B_0_30, itok_B_0_15, L0_cond_weights, L1_cond_weights):
    import numpy as np
    import concourse.bacc as bacc
    from concourse.bass_utils import run_bass_kernel_spmd

    nc = bacc.Bacc("TRN2", target_bir_lowering=False, num_devices=1)
    arrays, args = {}, []
    for name, a in (("x", x), ("subj", itok_B_0_30), ("cond", itok_B_0_15),
                    ("w0", L0_cond_weights), ("w1", L1_cond_weights)):
        arrays[name] = np.ascontiguousarray(a)
        args.append(nc.dram_tensor(name, arrays[name].shape, mybir.dt.from_np(arrays[name].dtype),
                                   kind="ExternalInput").ap())
    args.append(nc.dram_tensor("out", arrays["x"].shape, mybir.dt.float32, kind="ExternalOutput").ap())
    cond_resid_kernel(nc, *args)
    return run_bass_kernel_spmd(nc, [arrays], core_ids=[0]).results[0]["out"]
```

```python
import concourse.bass as bass
from concourse import mybir
from contextlib import ExitStack


def cond_resid_kernel(nc, x, subj, cond, w0, w1, out):
    f32 = mybir.dt.float32
    ALU = mybir.AluOpType
    ACT = mybir.ActivationFunctionType

    BATCH, C, T = x.shape
    S0, S1 = w0.shape[0], w1.shape[0]
    BANK = 512
    HALF = T // 2
    SLOTS = 16
    GROUP = 2
    GROUPS = SLOTS // GROUP
    TURNS = BATCH // SLOTS
    PER_BANK = BANK // C
    TGROUPS = S0 // PER_BANK
    W0_PARTS = 4
    PART = S0 // W0_PARTS
    assert C == 128 and HALF == 2 * BANK and BATCH == TURNS * SLOTS and S0 == TGROUPS * PER_BANK
    assert PART % PER_BANK == 0

    x_c = x.rearrange("b c t -> c b t")
    out_c = out.rearrange("b c t -> c b t")
    w0_c = w0.rearrange("s c d -> c s d")
    w1_c = w1.rearrange("s c d -> c s d")

    ctx = ExitStack()
    with ctx:
        def sb(name, shape, dt=f32):
            return ctx.enter_context(nc.sbuf_tensor(name, shape, dt))

        def sem(name):
            return ctx.enter_context(nc.semaphore(name))

        xs = sb("xs", [C, SLOTS, T])
        w0_sb = sb("w0_sb", [C, S0, C])
        w0T_sb = sb("w0T_sb", [C, S0, C])
        w1_sb = sb("w1_sb", [C, S1, C])
        subj_sb = sb("subj_sb", [1, BATCH], subj.dtype)
        cond_sb = sb("cond_sb", [1, BATCH], cond.dtype)
        ident = sb("ident", [C, C])
        aT = sb("aT", [C, 2, C])
        bw = sb("bw", [C, 2, C])
        ab_sum = sb("ab_sum", [C, 2, C])
        m = sb("m", [C, 2, C])

        ps_x = ctx.enter_context(nc.psum_tensor("ps_x", [C, 2, HALF], f32))
        ps_ab = ctx.enter_context(nc.psum_tensor("ps_ab", [C, 2, BANK], f32))

        idx_in = sem("idx_in")
        w0_in = [sem(f"w0_in{p}") for p in range(W0_PARTS)]
        w1_in = sem("w1_in")
        x_in = [sem(f"x_in{s}") for s in range(GROUPS)]
        x_out = [sem(f"x_out{s}") for s in range(GROUPS)]
        x_out_last = sem("x_out_last")
        ident_zero = sem("ident_zero")
        ident_done = sem("ident_done")
        turned = sem("turned")
        turned_out = sem("turned_out")
        picked = sem("picked")
        ab_done = sem("ab_done")
        m_done = sem("m_done")
        half_done = sem("half_done")
        half_added = sem("half_added")

        block = ctx.enter_context(nc.Block())

        @block.sync
        def _(sp):
            for p in range(W0_PARTS):
                sp.dma_start(w0_sb[:, p * PART:(p + 1) * PART, :],
                             w0_c[:, p * PART:(p + 1) * PART, :]).then_inc(w0_in[p], 16)
            sp.dma_start(w1_sb[:, :, :], w1_c).then_inc(w1_in, 16)
            for s in range(GROUPS):
                sp.dma_start(xs[:, s * GROUP:(s + 1) * GROUP, :],
                             x_c[:, s * GROUP:(s + 1) * GROUP, :]).then_inc(x_in[s], 16)
            with sp.Fori(1, TURNS) as t:
                for s in range(GROUPS):
                    sp.wait_ge(x_out[s], 16 * t)
                    src = x_c[:, bass.ds(t * SLOTS + s * GROUP, GROUP), :]
                    sp.dma_start(xs[:, s * GROUP:(s + 1) * GROUP, :], src).then_inc(x_in[s], 16)

        @block.gpsimd
        def _(pool):
            nc.gpsimd.memset(ident[:, :], 0.0).then_inc(ident_zero, 1)
            pool.wait_ge(ident_zero, 1)
            nc.gpsimd.affine_select(out=ident[:, :], in_=ident[:, :], compare_op=ALU.not_equal, fill=1.0, base=0,
                                    pattern=[[-1, C]], channel_multiplier=1).then_inc(ident_done, 1)

            def pick(b, k):
                i = pool.value_load(subj_sb[0:1, bass.ds(b, 1)], min_val=0, max_val=S0 - 1)
                j = pool.value_load(cond_sb[0:1, bass.ds(b, 1)], min_val=0, max_val=S1 - 1)
                a = w0_sb[:, bass.ds(i, 1), :].rearrange("c a d -> c (a d)")
                at = w0T_sb[:, bass.ds(i, 1), :].rearrange("c a d -> c (a d)")
                bb = w1_sb[:, bass.ds(j, 1), :].rearrange("c a d -> c (a d)")
                nc.gpsimd.tensor_copy(aT[:, k % 2, :], at).then_inc(picked, 1)
                nc.gpsimd.tensor_copy(bw[:, k % 2, :], bb).then_inc(picked, 1)
                nc.gpsimd.tensor_tensor(ab_sum[:, k % 2, :], a, bb, ALU.add).then_inc(picked, 1)

            pool.wait_ge(idx_in, 32)
            for p in range(W0_PARTS):
                pool.wait_ge(w0_in[p], 16)
            pool.wait_ge(w1_in, 16)
            pool.wait_ge(turned_out, TGROUPS)
            for k in range(2):
                pick(k, k)
            with pool.Fori(1, BATCH // 2) as u:
                for k in range(2):
                    pool.wait_ge(m_done, u * 2 + (k - 1))
                    pick(u * 2 + k, k)

        @block.tensor
        def _(pe):
            pe.wait_ge(ident_done, 1)
            for g in range(TGROUPS):
                first = g * PER_BANK
                if first % PART == 0:
                    pe.wait_ge(w0_in[first // PART], 16)
                if g >= 4:
                    pe.wait_ge(turned_out, g - 3)
                bank = ps_x[:, g // 2 % 2, g % 2 * BANK:(g % 2 + 1) * BANK]
                for n in range(PER_BANK):
                    last = nc.tensor.transpose(bank[:, n * C:(n + 1) * C], w0_sb[:, first + n, :], ident[:, :])
                last.then_inc(turned, 1)

            def product_ab(b, k):
                pe.wait_ge(picked, b * 3 + 3)
                nc.tensor.matmul(ps_ab[:, k % 2, 0:C], aT[:, k % 2, :], bw[:, k % 2, :],
                                 start=True, stop=True).then_inc(ab_done, 1)

            def product_x(t, s, first):
                b = t * SLOTS + s
                pe.wait_ge(m_done, b + 1)
                pe.wait_ge(x_in[s // GROUP], t * 16 + 16)
                for h in range(2):
                    if not (first and s == 0):
                        pe.wait_ge(half_added, b * 2 + (h - 1))
                    for n in range(2):
                        col = h * HALF + n * BANK
                        last = nc.tensor.matmul(ps_x[:, h, n * BANK:(n + 1) * BANK], m[:, s % 2, :],
                                                xs[:, s, col:col + BANK], start=True, stop=True)
                    last.then_inc(half_done, 1)

            def turn(t, first=False, final=False):
                for s in range(SLOTS):
                    if not (final and s == SLOTS - 1):
                        product_ab(t * SLOTS + (s + 1), s + 1)
                    product_x(t, s, first)

            pe.wait_ge(turned_out, TGROUPS)
            product_ab(0, 0)
            turn(0, first=True)
            with pe.Fori(1, TURNS - 1) as t:
                turn(t)
            turn(TURNS - 1, final=True)

        @block.vector
        def _(dve):
            def make_m(b, k, reused):
                dve.wait_ge(ab_done, b + 1)
                dve.wait_ge(picked, b * 3 + 3)
                if reused:
                    dve.wait_ge(half_done, b * 2 - 2)
                nc.vector.tensor_tensor(m[:, k % 2, :], ps_ab[:, k % 2, 0:C], ab_sum[:, k % 2, :],
                                        ALU.add).then_inc(m_done, 1)

            def add_x(t, s):
                b = t * SLOTS + s
                for h in range(2):
                    dve.wait_ge(half_done, b * 2 + (h + 1))
                    xh = xs[:, s, h * HALF:(h + 1) * HALF]
                    nc.vector.tensor_tensor(xh, ps_x[:, h, :], xh, ALU.add).then_inc(half_added, 1)

            def turn(t, first=False, final=False):
                for s in range(SLOTS):
                    if not (final and s == SLOTS - 1):
                        make_m(t * SLOTS + (s + 1), s + 1, reused=not (first and s == 0))
                    add_x(t, s)

            make_m(0, 0, reused=False)
            turn(0, first=True)
            with dve.Fori(1, TURNS - 1) as t:
                turn(t)
            turn(TURNS - 1, final=True)

        @block.scalar
        def _(act):
            act.dma_start(subj_sb[:, :], subj.rearrange("(a n) -> a n", a=1)).then_inc(idx_in, 16)
            act.dma_start(cond_sb[:, :], cond.rearrange("(a n) -> a n", a=1)).then_inc(idx_in, 16)
            for g in range(TGROUPS):
                act.wait_ge(turned, g + 1)
                bank = ps_x[:, g // 2 % 2, g % 2 * BANK:(g % 2 + 1) * BANK]
                dst = w0T_sb[:, g * PER_BANK:(g + 1) * PER_BANK, :].rearrange("c s d -> c (s d)")
                nc.scalar.activation(dst, bank, ACT.Copy).then_inc(turned_out, 1)

            def store(t, s):
                b = t * SLOTS + s * GROUP
                act.wait_ge(half_added, b * 2 + 2 * GROUP)
                act.dma_start(out_c[:, bass.ds(b, GROUP), :],
                              xs[:, s * GROUP:(s + 1) * GROUP, :]).then_inc(x_out[s], 16)

            with act.Fori(0, TURNS - 1) as t:
                for s in range(GROUPS):
                    store(t, s)
            for s in range(GROUPS - 1):
                store(TURNS - 1, s)
            for n in range(2 * (BATCH - GROUP), 2 * BATCH):
                b, h = n // 2, n % 2 * HALF
                act.wait_ge(half_added, n + 1)
                act.dma_start(out[b, :, h:h + HALF], xs[:, b % SLOTS, h:h + HALF]).then_inc(x_out_last, 16)
            for s in range(GROUPS - 1):
                act.wait_ge(x_out[s], 16 * TURNS)
            act.wait_ge(x_out[GROUPS - 1], 16 * (TURNS - 1))
            act.wait_ge(x_out_last, 16 * 2 * GROUP)


def kernel(x, itok_B_0_30, itok_B_0_15, L0_cond_weights, L1_cond_weights):
    import numpy as np
    import concourse.bacc as bacc
    from concourse.bass_utils import run_bass_kernel_spmd

    nc = bacc.Bacc("TRN2", target_bir_lowering=False, num_devices=1)
    arrays, args = {}, []
    for name, a in (("x", x), ("subj", itok_B_0_30), ("cond", itok_B_0_15),
                    ("w0", L0_cond_weights), ("w1", L1_cond_weights)):
        arrays[name] = np.ascontiguousarray(a)
        args.append(nc.dram_tensor(name, arrays[name].shape, mybir.dt.from_np(arrays[name].dtype),
                                   kind="ExternalInput").ap())
    args.append(nc.dram_tensor("out", arrays["x"].shape, mybir.dt.float32, kind="ExternalOutput").ap())
    cond_resid_kernel(nc, *args)
    return run_bass_kernel_spmd(nc, [arrays], core_ids=[0]).results[0]["out"]
```
